# Optimizing a Trainium2 kernel written in Bass

```python
import numpy as np
import jax
import jax.numpy as jnp

def _softmax(x, axis=-1):
    return jax.nn.softmax(x, axis=axis)

def _gelu(x):
    return jax.nn.gelu(x, approximate=True)

def _silu(x):
    return jax.nn.silu(x)

def _sigmoid(x):
    return jax.nn.sigmoid(x)

def _layernorm(x, axis=-1, eps=1e-05):
    m = jnp.mean(x, axis=axis, keepdims=True)
    v = jnp.var(x, axis=axis, keepdims=True)
    return (x - m) / jnp.sqrt(v + eps)

def _scatter_add(tgt, idx, src, axis=0):
    return tgt.at[idx].add(src)

def _segment_sum(src, seg, n):
    return jax.ops.segment_sum(src, seg, n)
kernel_name = 'mk_gnn_preln_d4_gnn_r16_561a47'

def setup_inputs(seed: int=0):
    np.random.seed(seed)
    _w = jnp.asarray

    def _rec_inputs():
        import jax
        import jax.numpy as jnp
        _gk = jax.random.key(seed)
        x = -1.749e-05 + 0.08837 * jax.random.normal(jax.random.fold_in(_gk, 1), (6250, 128), jnp.float32)
        src = jax.random.randint(jax.random.fold_in(_gk, 2), (200000,), 0, 6250, jnp.int32)
        dst = jnp.minimum((6250 * jax.random.uniform(jax.random.fold_in(_gk, 3), (200000,)) ** 2.0).astype(jnp.int32), 99999)
        _o = jnp.argsort(dst, stable=True)
        src = src[_o]
        dst = dst[_o]
        edge_attr_17 = -0.000119442 + 0.999915 * jax.random.normal(jax.random.fold_in(_gk, 12), (200000, 17), jnp.float32)
        edge_type_16 = jax.random.randint(jax.random.fold_in(_gk, 14), (200000,), 0, 16, jnp.int32)
        node_type_8 = jax.random.randint(jax.random.fold_in(_gk, 15), (6250,), 0, 8, jnp.int32)
        return (x, src, dst, edge_attr_17, edge_type_16, node_type_8)
    x, src, dst, edge_attr_17, edge_type_16, node_type_8 = _rec_inputs()

    def _L0_gnn_setup():
        import jax, jax.numpy as jnp
        import numpy as np
        N, E, D, H, C = (3125, 50000, 128, 4, 32)

        def _gat_conv(x, src, dst, W, a_src, a_dst, b, concat):
            n = x.shape[0]
            h, c = a_src.shape
            xl = (x @ W).reshape(n, h, c)
            a_s = (xl * a_src).sum(-1)
            a_d = (xl * a_dst).sum(-1)
            logits = jax.nn.leaky_relu(a_s[src] + a_d[dst], negative_slope=0.2)
            m = jax.ops.segment_max(logits, dst, num_segments=n)
            e = jnp.exp(logits - m[dst])
            denom = jax.ops.segment_sum(e, dst, num_segments=n)
            alpha = e / (denom[dst] + 1e-16)
            msg = xl[src] * alpha[:, :, None]
            out = jax.ops.segment_sum(msg, dst, num_segments=n)
            out = out.reshape(n, h * c) if concat else out.mean(axis=1)
            return out + b
        key = jax.random.key(seed)
        ks = jax.random.split(key, 9)
        s = 1.0 / np.sqrt(D)
        return {'edge_index': jax.random.randint(ks[0], (2, E), 0, N), 'emb': jax.random.normal(ks[1], (N, D), dtype=jnp.float32) * s, 'W1': jax.random.normal(ks[2], (D, H * C), dtype=jnp.float32) * s, 'att_src1': jax.random.normal(ks[3], (H, C), dtype=jnp.float32) * s, 'att_dst1': jax.random.normal(ks[4], (H, C), dtype=jnp.float32) * s, 'b1': jnp.zeros((H * C,), dtype=jnp.float32), 'W2': jax.random.normal(ks[5], (D, D), dtype=jnp.float32) * s, 'att_src2': jax.random.normal(ks[6], (1, D), dtype=jnp.float32) * s, 'att_dst2': jax.random.normal(ks[7], (1, D), dtype=jnp.float32) * s, 'b2': jnp.zeros((D,), dtype=jnp.float32)}
    _L0_gnn_all = _L0_gnn_setup()
    _L0_gnn_in = {k: v for k, v in _L0_gnn_all.items() if k in ('W1', 'att_src1', 'att_dst1', 'b1', 'W2', 'att_src2', 'att_dst2', 'b2')}
    del _L0_gnn_all

    def _L1_gnn_setup():
        import jax, jax.numpy as jnp
        import numpy as np
        N_NODES = 3125
        N_EDGES = 50000
        IN_DIM = 128
        OUT_DIM = 128
        EDGE_DIM = 17
        BN_EPS = 1e-05

        def _prelu(x, a):
            return jnp.where(x >= 0, x, a * x)
        key = jax.random.key(seed)
        ks = jax.random.split(key, 12)

        def lin(k, fan_in, shape):
            bound = 1.0 / np.sqrt(fan_in)
            return jax.random.uniform(k, shape, jnp.float32, -bound, bound)
        return {'node_feats': jax.random.normal(ks[0], (N_NODES, IN_DIM), jnp.float32), 'edge_feats': jax.random.normal(ks[1], (N_EDGES, EDGE_DIM), jnp.float32), 'src_idx': jax.random.randint(ks[2], (N_EDGES,), 0, N_NODES), 'dst_idx': jax.random.randint(ks[3], (N_EDGES,), 0, N_NODES), 'W_src': lin(ks[4], IN_DIM, (OUT_DIM, IN_DIM)), 'b_src': lin(ks[5], IN_DIM, (OUT_DIM,)), 'W_dst': lin(ks[6], IN_DIM, (OUT_DIM, IN_DIM)), 'b_dst': lin(ks[7], IN_DIM, (OUT_DIM,)), 'W_edge': lin(ks[8], EDGE_DIM, (OUT_DIM, EDGE_DIM)), 'b_edge': lin(ks[9], EDGE_DIM, (OUT_DIM,)), 'prelu_a': jnp.float32(0.25), 'gamma': jnp.ones((OUT_DIM,), jnp.float32), 'beta': jnp.zeros((OUT_DIM,), jnp.float32)}
    _L1_gnn_all = _L1_gnn_setup()
    _L1_gnn_in = {k: v for k, v in _L1_gnn_all.items() if k in ('W_src', 'b_src', 'W_dst', 'b_dst', 'W_edge', 'b_edge', 'prelu_a', 'gamma', 'beta')}
    del _L1_gnn_all

    def _L2_gnn_setup():
        import math
        import jax, jax.numpy as jnp
        import numpy as np
        N, E = (2500, 40000)
        IN, OUT, T, R, H = (128, 128, 8, 16, 8)
        DK = OUT // H

        def _tproj(x, W, types):
            allp = jnp.einsum('ni,tio->nto', x, W)
            return jnp.take_along_axis(allp, types[:, None, None], axis=1)[:, 0]
        if __name__ == '__main__':
            inp = setup_inputs()
            o = reference(**inp)
            print(o.shape, o.dtype)
        key = jax.random.key(seed)
        ks = jax.random.split(key, 12)
        h = jax.random.normal(ks[0], (N, IN), jnp.float32)
        src = jax.random.randint(ks[1], (E,), 0, N)
        dst = jax.random.randint(ks[2], (E,), 0, N)
        ntype = jax.random.randint(ks[3], (N,), 0, T)
        etype = jax.random.randint(ks[4], (E,), 0, R)
        s = 0.05
        k_weight = jax.random.uniform(ks[5], (T, IN, OUT), jnp.float32) * s
        q_weight = jax.random.uniform(ks[6], (T, IN, OUT), jnp.float32) * s
        v_weight = jax.random.uniform(ks[7], (T, IN, OUT), jnp.float32) * s
        a_weight = jax.random.uniform(ks[8], (T, OUT, OUT), jnp.float32) * s
        relation_att = jax.random.uniform(ks[9], (R, H, DK, DK), jnp.float32) * s
        relation_msg = jax.random.uniform(ks[10], (R, H, DK, DK), jnp.float32) * s
        relation_pri = jnp.ones((R, H), jnp.float32)
        skip = jnp.ones((T, H), jnp.float32)
        return dict(h=h, k_weight=k_weight, q_weight=q_weight, v_weight=v_weight, a_weight=a_weight, relation_pri=relation_pri, relation_att=relation_att, relation_msg=relation_msg, skip=skip, src=src, dst=dst, ntype=ntype, etype=etype)
    _L2_gnn_all = _L2_gnn_setup()
    _L2_gnn_in = {k: v for k, v in _L2_gnn_all.items() if k in ('k_weight', 'q_weight', 'v_weight', 'a_weight', 'relation_pri', 'relation_att', 'relation_msg', 'skip')}
    del _L2_gnn_all

    def _L3_gnn_setup():
        import jax, jax.numpy as jnp
        import numpy as np
        N = 6250
        IN_DIM = 128
        OUT_DIM = 128
        E = 200000
        key = jax.random.key(seed)
        k1, k2, k3, k4, k5 = jax.random.split(key, 5)
        x = jax.random.normal(k1, (N, IN_DIM), dtype=jnp.float32)
        src = jax.random.randint(k2, (E,), 0, N)
        dst = jax.random.randint(k3, (E,), 0, N)
        edge_index = jnp.stack([src, dst], axis=0)
        bound = 1.0 / np.sqrt(2 * IN_DIM)
        W = jax.random.uniform(k4, (OUT_DIM, 2 * IN_DIM), minval=-bound, maxval=bound, dtype=jnp.float32)
        b = jax.random.uniform(k5, (OUT_DIM,), minval=-bound, maxval=bound, dtype=jnp.float32)
        return {'x': x, 'edge_index': edge_index, 'W': W, 'b': b}
    _L3_gnn_all = _L3_gnn_setup()
    _L3_gnn_in = {k: v for k, v in _L3_gnn_all.items() if k in ('W', 'b')}
    del _L3_gnn_all
    return {'x': x, 'src': src, 'dst': dst, 'edge_attr_17': edge_attr_17, 'edge_type_16': edge_type_16, 'node_type_8': node_type_8, 'L0_gnn_W1': _L0_gnn_in['W1'], 'L0_gnn_att_src1': _L0_gnn_in['att_src1'], 'L0_gnn_att_dst1': _L0_gnn_in['att_dst1'], 'L0_gnn_b1': _L0_gnn_in['b1'], 'L0_gnn_W2': _L0_gnn_in['W2'], 'L0_gnn_att_src2': _L0_gnn_in['att_src2'], 'L0_gnn_att_dst2': _L0_gnn_in['att_dst2'], 'L0_gnn_b2': _L0_gnn_in['b2'], 'L1_gnn_W_src': _L1_gnn_in['W_src'], 'L1_gnn_b_src': _L1_gnn_in['b_src'], 'L1_gnn_W_dst': _L1_gnn_in['W_dst'], 'L1_gnn_b_dst': _L1_gnn_in['b_dst'], 'L1_gnn_W_edge': _L1_gnn_in['W_edge'], 'L1_gnn_b_edge': _L1_gnn_in['b_edge'], 'L1_gnn_prelu_a': _L1_gnn_in['prelu_a'], 'L1_gnn_gamma': _L1_gnn_in['gamma'], 'L1_gnn_beta': _L1_gnn_in['beta'], 'L2_gnn_k_weight': _L2_gnn_in['k_weight'], 'L2_gnn_q_weight': _L2_gnn_in['q_weight'], 'L2_gnn_v_weight': _L2_gnn_in['v_weight'], 'L2_gnn_a_weight': _L2_gnn_in['a_weight'], 'L2_gnn_relation_pri': _L2_gnn_in['relation_pri'], 'L2_gnn_relation_att': _L2_gnn_in['relation_att'], 'L2_gnn_relation_msg': _L2_gnn_in['relation_msg'], 'L2_gnn_skip': _L2_gnn_in['skip'], 'L3_gnn_W': _L3_gnn_in['W'], 'L3_gnn_b': _L3_gnn_in['b']}

def reference(x, src, dst, edge_attr_17, edge_type_16, node_type_8, L0_gnn_W1, L0_gnn_att_src1, L0_gnn_att_dst1, L0_gnn_b1, L0_gnn_W2, L0_gnn_att_src2, L0_gnn_att_dst2, L0_gnn_b2, L1_gnn_W_src, L1_gnn_b_src, L1_gnn_W_dst, L1_gnn_b_dst, L1_gnn_W_edge, L1_gnn_b_edge, L1_gnn_prelu_a, L1_gnn_gamma, L1_gnn_beta, L2_gnn_k_weight, L2_gnn_q_weight, L2_gnn_v_weight, L2_gnn_a_weight, L2_gnn_relation_pri, L2_gnn_relation_att, L2_gnn_relation_msg, L2_gnn_skip, L3_gnn_W, L3_gnn_b):
    import jax
    import jax.numpy as jnp

    def _L0_gnn_ref(edge_index, emb, W1, att_src1, att_dst1, b1, W2, att_src2, att_dst2, b2):
        import jax, jax.numpy as jnp
        import numpy as np
        N, E, D, H, C = (3125, 50000, 128, 4, 32)

        def _gat_conv(x, src, dst, W, a_src, a_dst, b, concat):
            n = x.shape[0]
            h, c = a_src.shape
            xl = (x @ W).reshape(n, h, c)
            a_s = (xl * a_src).sum(-1)
            a_d = (xl * a_dst).sum(-1)
            logits = jax.nn.leaky_relu(a_s[src] + a_d[dst], negative_slope=0.2)
            m = jax.ops.segment_max(logits, dst, num_segments=n)
            e = jnp.exp(logits - m[dst])
            denom = jax.ops.segment_sum(e, dst, num_segments=n)
            alpha = e / (denom[dst] + 1e-16)
            msg = xl[src] * alpha[:, :, None]
            out = jax.ops.segment_sum(msg, dst, num_segments=n)
            out = out.reshape(n, h * c) if concat else out.mean(axis=1)
            return out + b
        n = emb.shape[0]
        loop = jnp.arange(n)
        src = jnp.concatenate([edge_index[0], loop])
        dst = jnp.concatenate([edge_index[1], loop])
        x = _gat_conv(emb, src, dst, W1, att_src1, att_dst1, b1, True)
        x = jax.nn.elu(x)
        x = _gat_conv(x, src, dst, W2, att_src2, att_dst2, b2, False)
        return x / jnp.maximum(jnp.linalg.norm(x, axis=1, keepdims=True), 1e-12)

    def _L1_gnn_ref(node_feats, edge_feats, src_idx, dst_idx, W_src, b_src, W_dst, b_dst, W_edge, b_edge, prelu_a, gamma, beta):
        import jax, jax.numpy as jnp
        import numpy as np
        N_NODES = 3125
        N_EDGES = 50000
        IN_DIM = 128
        OUT_DIM = 128
        EDGE_DIM = 17
        BN_EPS = 1e-05

        def _prelu(x, a):
            return jnp.where(x >= 0, x, a * x)
        n_nodes = node_feats.shape[0]
        h_src = node_feats @ W_src.T + b_src
        h_dst = node_feats @ W_dst.T + b_dst
        e_proj = edge_feats @ W_edge.T + b_edge
        z = h_src[src_idx] + h_dst[dst_idx] + e_proj
        z = _prelu(z, prelu_a)
        h_new = jax.ops.segment_sum(z, dst_idx, num_segments=n_nodes)
        mean = jnp.mean(h_new, axis=0)
        var = jnp.mean(jnp.square(h_new - mean), axis=0)
        h_bn = (h_new - mean) * jax.lax.rsqrt(var + BN_EPS) * gamma + beta
        out = _prelu(h_bn, prelu_a)
        return out

    def _L2_gnn_ref(h, k_weight, q_weight, v_weight, a_weight, relation_pri, relation_att, relation_msg, skip, src, dst, ntype, etype):
        import math
        import jax, jax.numpy as jnp
        import numpy as np
        N, E = (2500, 40000)
        IN, OUT, T, R, H = (128, 128, 8, 16, 8)
        DK = OUT // H

        def _tproj(x, W, types):
            allp = jnp.einsum('ni,tio->nto', x, W)
            return jnp.take_along_axis(allp, types[:, None, None], axis=1)[:, 0]
        if __name__ == '__main__':
            inp = setup_inputs()
            o = reference(**inp)
            print(o.shape, o.dtype)
        n, _ = h.shape
        nT, _, out = k_weight.shape
        nR, nH, dk, _ = relation_att.shape
        e = src.shape[0]
        sqrt_dk = math.sqrt(out)
        k_n = _tproj(h, k_weight, ntype)
        v_n = _tproj(h, v_weight, ntype)
        q_n = _tproj(h, q_weight, ntype)
        k = k_n[src].reshape(e, nH, dk)
        v = v_n[src].reshape(e, nH, dk)
        q = q_n[dst].reshape(e, nH, dk)
        k2 = jnp.zeros_like(k)
        v2 = jnp.zeros_like(v)
        for r in range(nR):
            m = (etype == r)[:, None, None]
            k2 = k2 + jnp.where(m, jnp.einsum('ehd,hdc->ehc', k, relation_att[r]), 0.0)
            v2 = v2 + jnp.where(m, jnp.einsum('ehd,hdc->ehc', v, relation_msg[r]), 0.0)
        attn = jnp.einsum('ehd,ehd->eh', k2, q) * relation_pri[etype] / sqrt_dk
        amax = jax.lax.stop_gradient(jax.ops.segment_max(attn, dst, num_segments=n))
        p = jnp.exp(attn - amax[dst])
        denom = jax.ops.segment_sum(p, dst, num_segments=n)
        alpha = p / denom[dst]
        msg = alpha[:, :, None] * v2
        t = jax.ops.segment_sum(msg.reshape(e, nH * dk), dst, num_segments=n)
        trans = _tproj(t, a_weight, ntype)
        gate = jax.nn.sigmoid(skip[ntype])
        out_h = (trans.reshape(n, nH, dk) * gate[:, :, None]).reshape(n, out)
        return out_h

    def _L3_gnn_ref(x, edge_index, W, b):
        import jax, jax.numpy as jnp
        import numpy as np
        N = 6250
        IN_DIM = 128
        OUT_DIM = 128
        E = 200000
        n = x.shape[0]
        src, dst = (edge_index[0], edge_index[1])
        agg = jax.ops.segment_sum(x[src], dst, num_segments=n)
        count = jax.ops.segment_sum(jnp.ones((src.shape[0],), x.dtype), dst, num_segments=n)
        count = jnp.maximum(count, 1.0)[:, None]
        neigh_mean = agg / count
        combined = jnp.concatenate([x, neigh_mean], axis=1)
        return combined @ W.T + b
    edge_index = jnp.stack([src, dst])
    h = jnp.maximum(_layernorm(x, axis=-1), 0.0)
    x = x + _L0_gnn_ref(edge_index, h, L0_gnn_W1, L0_gnn_att_src1, L0_gnn_att_dst1, L0_gnn_b1, L0_gnn_W2, L0_gnn_att_src2, L0_gnn_att_dst2, L0_gnn_b2)
    h = jnp.maximum(_layernorm(x, axis=-1), 0.0)
    x = x + _L1_gnn_ref(h, edge_attr_17, src, dst, L1_gnn_W_src, L1_gnn_b_src, L1_gnn_W_dst, L1_gnn_b_dst, L1_gnn_W_edge, L1_gnn_b_edge, L1_gnn_prelu_a, L1_gnn_gamma, L1_gnn_beta)
    h = jnp.maximum(_layernorm(x, axis=-1), 0.0)
    x = x + _L2_gnn_ref(h, L2_gnn_k_weight, L2_gnn_q_weight, L2_gnn_v_weight, L2_gnn_a_weight, L2_gnn_relation_pri, L2_gnn_relation_att, L2_gnn_relation_msg, L2_gnn_skip, src, dst, node_type_8, edge_type_16)
    h = jnp.maximum(_layernorm(x, axis=-1), 0.0)
    x = x + _L3_gnn_ref(h, edge_index, L3_gnn_W, L3_gnn_b)
    return x

_drawn_inputs = setup_inputs


def setup_inputs(seed=0):
    import zlib

    import numpy as np

    out = dict(_drawn_inputs(seed))
    spreads = {'L0_gnn_b1': (0.0, 0.1),
     'L0_gnn_b2': (0.0, 0.1),
     'L1_gnn_gamma': (1.0, 0.2),
     'L1_gnn_beta': (0.0, 0.1),
     'L2_gnn_relation_pri': (1.0, 0.2),
     'L2_gnn_skip': (1.0, 0.2)}
    factors = {}
    for name, (base, spread) in spreads.items():
        noise = np.random.default_rng([zlib.crc32(name.encode()), seed]).standard_normal(out[name].shape)
        drawn = base * np.exp(spread * noise) if base else spread * noise
        out[name] = jnp.asarray(drawn.astype(out[name].dtype))
    for name, factor in factors.items():
        out[name] = (out[name] * factor).astype(out[name].dtype)
    return out
```

```python
from contextlib import ExitStack

import numpy as np

import concourse.bass as bass
from concourse import mybir

ALU = mybir.AluOpType
ACT = mybir.ActivationFunctionType
AX = mybir.AxisListType
F32 = mybir.dt.float32
I32 = mybir.dt.int32

P = 128
N = 6250
E = 200000
D = 128
NODE_TILES = -(-N // P)
TAIL = N - (NODE_TILES - 1) * P
NT = NODE_TILES + 1
NP = NT * P
G = 2
EB = G * P
NB = -(-E // EB)
U = 4
V = U * G
STEPS = -(-(NB + NODE_TILES - 1) // (2 * U)) * (2 * U)
NI = STEPS // U
ST = 104
NST = STEPS // ST
assert NST * ST == STEPS and ST % U == 0 and ST <= P
IPT = ST // U
GT = 5
NG = NT // GT
TYPES = 8
RELS = 16
ATTRS = 17
BIG = 1.0e30
LN_EPS = 1e-5
PAD_DST = 1 << 20
ROW = 264


def build(nc, src_rows, dst_rows, etype_rows, attr_t, x, node_type, W1, att_src1, att_dst1, b1, W2, att_src2,
          att_dst2, b2, w_src_t, b_src, w_dst_t, b_dst, w_edge_t, b_edge, prelu_a, gamma, beta, k_w, q_w, v_w,
          a_w, pri, rel_att, rel_msg, skip, W3_t, b3, W1_t, W2_t, out):
    ctx = ExitStack()
    with ctx:
        def sb(name, shape, dt=F32):
            return ctx.enter_context(nc.sbuf_tensor(name, shape, dt))

        phase = {"ctx": ExitStack(), "sems": []}

        def sem(name):
            s = phase["ctx"].enter_context(nc.semaphore(name))
            phase["sems"].append(s)
            return s

        X = sb("X", [P, NT, D])
        Y = sb("Y", [P, NT, D])
        LK = sb("LK", [P, NT, D])
        ACC = sb("ACC", [P, NT * 136])
        MX = sb("MX", [P, NT, 8])
        src_c = sb("src_c", [P, NI * V], I32)
        rel_c = sb("rel_c", [P, NI * V], I32)
        dst_c = sb("dst_c", [P, NI * V])
        tile_row = sb("tile_row", [1, STEPS], I32)
        block_row = sb("block_row", [1, STEPS], I32)
        iota = sb("iota", [P, P])
        iota_p = sb("iota_p", [P, 1])
        ident = sb("ident", [P, P])
        ones = sb("ones", [P, P])
        mean = sb("mean", [P, NT])
        rstd = sb("rstd", [P, NT])
        work = sb("work", [P, 19640])

        def carve(specs):
            at, found = 0, {}
            for name, cols in specs:
                found[name] = work[:, at:at + cols]
                at += cols
            assert at <= 19640, at
            return found

        psum = [ctx.enter_context(nc.psum_tensor(f"ps{i}", [P, 1024], F32)) for i in range(4)]

        tab_132 = nc.dram_tensor("tab_gat1", [NP, 136], F32, kind="Internal").ap()
        tab_129 = nc.dram_tensor("tab_gat2", [NP, 130], F32, kind="Internal").ap()
        tab_sum = nc.dram_tensor("tab_sum", [NP, 128], F32, kind="Internal").ap()
        tab_rel = nc.dram_tensor("tab_rel", [NP * RELS, 264], F32, kind="Internal").ap()
        tab_mean = nc.dram_tensor("tab_mean", [NP, 129], F32, kind="Internal").ap()

        parts = {"sync": [], "gpsimd": [], "scalar": [], "vector": [], "tensor": []}

        def part(engine):
            def add(fn):
                parts[engine].append(fn)
                return fn
            return add

        def wait(e, s, v):
            if isinstance(v, int) and v <= 0:
                return
            e.wait_ge(s, v)

        def swdge_sem(name):
            return ctx.enter_context(nc.semaphore(name))

        s_met = ctx.enter_context(nc.semaphore("s_met"))
        s_cleared = ctx.enter_context(nc.semaphore("s_cleared"))
        met = [0]

        def move(e, to, of):
            return e.tensor_scalar(to, of, 1.0, None, ALU.mult)

        def meeting():
            met[0] += 1
            k, sems = met[0], phase["sems"]

            def other(e):
                e.sem_inc(s_met, 1)
                e.wait_ge(s_cleared, k)

            def clearing(e):
                e.wait_ge(s_met, (len(parts) - 1) * k)
                for s in sems:
                    e.sem_clear(s)
                e.sem_inc(s_cleared, 1)
            for eng in parts:
                parts[eng].append(clearing if eng == "gpsimd" else other)
            phase["ctx"].close()
            phase["ctx"], phase["sems"] = ExitStack(), []

        s_iota = sem("s_iota")
        s_const = sem("s_const")
        s_x = sem("s_x")

        @part("gpsimd")
        def _(e):
            e.iota(iota[:, :], pattern=[[1, P]], base=0, channel_multiplier=0,
                   allow_small_or_imprecise_dtypes=True).then_inc(s_iota, 1)
            e.iota(iota_p[:, :], pattern=[[0, 1]], base=0, channel_multiplier=1,
                   allow_small_or_imprecise_dtypes=True).then_inc(s_iota, 1)
            e.memset(ones[:, :], 1.0).then_inc(s_iota, 1)

        @part("vector")
        def _(e):
            e.wait_ge(s_iota, 3)
            e.tensor_scalar(ident[:, :], iota[:, :], iota_p[:, 0:1], None, ALU.is_equal).then_inc(s_const, 1)
            e.wait_ge(s_const, 1)

        @part("tensor")
        def _(e):
            e.wait_ge(s_const, 1)

        @part("sync")
        def _(e):
            e.dma_start(X[:, :, :], x).then_inc(s_x, 16)
            e.wait_ge(s_x, 16)

        w = carve([("first", NB), ("last", NB), ("cnt", 8), ("lt", NB), ("krow", STEPS), ("ge0", STEPS),
                   ("ge1", STEPS), ("upper", P), ("kcol", 8), ("bcol", NST), ("tcol", NST), ("bidx", NST),
                   ("thr", 2), ("rows", 3 * EB), ("rowsf", 3 * EB), ("c128", 1), ("brow", STEPS), ("fl", 2 * NB)])
        s_fl = sem("s_first_last")
        s_kio = sem("s_step_iota")
        vS = sem("v_steps")
        pS0 = sem("p_steps")
        s_rows = swdge_sem("s_step_rows")
        vR = sem("v_step_rows")
        pR0 = sem("p_step_rows")
        NTT = NODE_TILES
        flrow = w["fl"][0:1, :].rearrange("p (a b) -> p a b", a=2)

        @part("sync")
        def _(e, w=w):
            e.dma_start(flrow[:, 0, :].bitcast(I32), dst_rows[:, 0:1].rearrange("b o -> o b"),
                        allow_slow_non_contiguous=True).then_inc(s_fl, 16)
            e.dma_start(flrow[:, 1, :].bitcast(I32), dst_rows[:, EB - 1:EB].rearrange("b o -> o b"),
                        allow_slow_non_contiguous=True).then_inc(s_fl, 16)

        @part("gpsimd")
        def _(e, w=w):
            e.iota(w["krow"], pattern=[[1, STEPS]], base=0, channel_multiplier=0,
                   allow_small_or_imprecise_dtypes=True).then_inc(s_kio, 1)
            e.iota(w["kcol"][:, 0:NST], pattern=[[ST, NST]], base=0, channel_multiplier=1,
                   allow_small_or_imprecise_dtypes=True).then_inc(s_kio, 1)

        halves = [(0, 512), (512, NB)]
        khalves = [(0, 512), (512, STEPS)]

        @part("vector")
        def _(e, w=w):
            n = [0]

            def done(ins):
                n[0] += 1
                ins.then_inc(vS, 1)
                e.wait_ge(vS, n[0])
            e.wait_ge(s_fl, 32)
            e.wait_ge(s_kio, 2)
            done(e.tensor_copy(w["first"][0:1, :], flrow[:, 0, :].bitcast(I32)))
            done(e.tensor_copy(w["last"][0:1, :], flrow[:, 1, :].bitcast(I32)))
            done(e.tensor_scalar(w["upper"], iota[:, :], iota_p[:, 0:1], None, ALU.is_gt))
            done(e.tensor_scalar(w["thr"][:, 0:1], iota_p[:, :], float(P), None, ALU.mult))
            done(e.tensor_scalar(w["thr"][:, 1:2], iota_p[:, :], float(P), float(P), ALU.mult, ALU.add))
            done(e.memset(w["c128"], float(P)))
            e.wait_ge(pS0, 1)
            T = slice(0, NTT)
            cnt = w["cnt"]
            done(e.tensor_scalar(w["lt"][T, :], psum[1][T, 0:NB], w["thr"][T, 0:1], None, ALU.is_lt))
            done(e.tensor_reduce(cnt[T, 0:1], w["lt"][T, :], AX.X, ALU.add))
            done(e.tensor_scalar(w["lt"][T, :], psum[0][T, 0:NB], w["thr"][T, 1:2], None, ALU.is_lt))
            done(e.tensor_reduce(cnt[T, 1:2], w["lt"][T, :], AX.X, ALU.add))
            done(e.tensor_tensor(cnt[T, 2:3], cnt[T, 1:2], cnt[T, 0:1], ALU.subtract))
            done(e.tensor_scalar(cnt[T, 2:3], cnt[T, 2:3], 1.0, None, ALU.max))
            e.wait_ge(pS0, 2)
            done(e.tensor_copy(cnt[T, 3:4], psum[2][T, 0:1]))
            done(e.tensor_tensor(cnt[T, 4:5], cnt[T, 3:4], cnt[T, 2:3], ALU.add))
            done(e.tensor_tensor(cnt[T, 5:6], cnt[T, 0:1], cnt[T, 3:4], ALU.subtract))
            done(e.tensor_scalar(w["ge0"][T, :], w["krow"][T, :], cnt[T, 3:4], None, ALU.is_ge))
            done(e.tensor_scalar(w["ge1"][T, :], w["krow"][T, :], cnt[T, 4:5], None, ALU.is_ge))
            done(e.tensor_tensor(w["ge0"][T, :], w["ge0"][T, :], w["ge1"][T, :], ALU.subtract))
            e.wait_ge(pS0, 3)
            done(e.tensor_copy(tile_row[:, :], psum[0][0:1, 0:STEPS]))
            done(e.tensor_tensor(w["brow"][0:1, :], psum[1][0:1, 0:STEPS], w["krow"][0:1, :], ALU.add))
            done(e.tensor_scalar(block_row[:, :], w["brow"][0:1, :], float(NB - 1), None, ALU.min))
            S = slice(0, ST)
            done(e.tensor_tensor(w["bcol"][S, :], psum[2][S, 0:NST], w["kcol"][S, 0:NST], ALU.add))
            done(e.tensor_scalar(w["bidx"][S, :].bitcast(I32), w["bcol"][S, :], float(NB - 1), None, ALU.min))
            done(e.tensor_copy(w["tcol"][S, :], psum[2][S, 512:512 + NST]))
            rows = w["rows"].rearrange("p (a b) -> p a b", a=3)
            rf = w["rowsf"].rearrange("p (a b) -> p a b", a=3)
            m = [0]

            def link(ins):
                m[0] += 1
                ins.then_inc(vR, 1)
                e.wait_ge(vR, m[0])
            for j in range(NST):
                e.wait_ge(s_rows, 48 * (j + 1))
                link(e.tensor_copy(rf[S, 0, :], rows[S, 0, :].bitcast(I32)))
                link(e.tensor_scalar(rf[S, 1, :], rows[S, 1, :].bitcast(I32), w["tcol"][S, j:j + 1], None,
                                     ALU.subtract))
                link(e.tensor_copy(rf[S, 2, :], rows[S, 2, :].bitcast(I32)))
                link(e.scalar_tensor_tensor(rf[S, 2, :], rf[S, 0, :], float(RELS), rf[S, 2, :],
                                            ALU.mult, ALU.add))
                e.wait_ge(pR0, j + 1)
                for a, to in ((0, src_c), (1, dst_c), (2, rel_c)):
                    for g in range(G):
                        c = (a * G + g) * P
                        v4 = to[:, :].rearrange("p (n g u) -> p n g u", g=G, u=U)
                        link(e.tensor_copy(v4[:, j * IPT:(j + 1) * IPT, g, :],
                                           psum[3][:, c:c + ST].rearrange("p (n u) -> p n u", u=U)))

        @part("tensor")
        def _(e, w=w):
            e.wait_ge(vS, 2)
            for k, name in ((0, "first"), (1, "last")):
                for a, b in halves:
                    ins = e.matmul(psum[k][0:NTT, a:b], ones[0:1, 0:NTT], w[name][0:1, a:b], start=True, stop=True)
            ins.then_inc(pS0, 1)
            e.wait_ge(vS, 12)
            e.matmul(psum[2][0:NTT, 0:1], w["upper"][0:NTT, 0:NTT], w["cnt"][0:NTT, 2:3],
                     start=True, stop=True).then_inc(pS0, 1)
            e.wait_ge(vS, 18)
            for a, b in khalves:
                e.matmul(psum[0][0:1, a:b], ones[0:NTT, 0:1], w["ge1"][0:NTT, a:b], start=True, stop=True)
                e.matmul(psum[1][0:1, a:b], w["cnt"][0:NTT, 5:6], w["ge0"][0:NTT, a:b], start=True, stop=True)
            for j in range(NST):
                e.matmul(psum[2][0:ST, j:j + 1], w["ge0"][0:NTT, j * ST:(j + 1) * ST], w["cnt"][0:NTT, 5:6],
                         start=True, stop=True)
                ins = e.matmul(psum[2][0:ST, 512 + j:513 + j], w["ge1"][0:NTT, j * ST:(j + 1) * ST],
                               w["c128"][0:NTT, :], start=True, stop=True)
            ins.then_inc(pS0, 1)
            for j in range(NST):
                e.wait_ge(vR, 10 * j + 4)
                for a in range(3):
                    for g in range(G):
                        c = (a * G + g) * P
                        ins = e.transpose(psum[3][:, c:c + ST],
                                          w["rowsf"][0:ST, a * EB + g * P:a * EB + (g + 1) * P], ident[0:ST, 0:ST])
                ins.then_inc(pR0, 1)

        @part("gpsimd")
        def _(e, w=w):
            e.wait_ge(vS, 24)
            for j in range(NST):
                if j:
                    e.wait_ge(vR, 10 * (j - 1) + 4)
                for a, rows in enumerate((src_rows, dst_rows, etype_rows)):
                    e.indirect_dma_start(w["rows"][0:ST, a * EB:(a + 1) * EB].bitcast(I32), None, rows,
                                         bass.IndirectOffsetOnAxis(ap=w["bidx"][0:ST, j:j + 1].bitcast(I32), axis=0)
                                         ).then_inc(s_rows, 16)

        def square_root(at, ap, s_before, count):
            s = sem(f"a_sqrt_{at}")

            @part("scalar")
            def _(e):
                e.wait_ge(s_before, count)
                e.activation(ap, ap, ACT.Sqrt).then_inc(s, 1)
            return s

        def layer_norm(name):
            vL = sem(f"v_{name}_norm")
            a_norm = square_root(name, rstd[:, :], vL, 6)

            @part("vector")
            def _(e):
                n = [0]

                def done(ins):
                    n[0] += 1
                    ins.then_inc(vL, 1)
                    e.wait_ge(vL, n[0])
                mb = mean[:, :].unsqueeze(2).to_broadcast([P, NT, D])
                done(e.tensor_reduce(mean[:, :], X[:, :, :], AX.X, ALU.add))
                done(e.tensor_scalar(mean[:, :], mean[:, :], 1.0 / D, None, ALU.mult))
                done(e.tensor_tensor(Y[:, :, :], X[:, :, :], mb, ALU.subtract))
                done(e.tensor_tensor(LK[:, :, :], Y[:, :, :], Y[:, :, :], ALU.mult))
                done(e.tensor_reduce(rstd[:, :], LK[:, :, :], AX.X, ALU.add))
                done(e.tensor_scalar(rstd[:, :], rstd[:, :], 1.0 / D, LN_EPS, ALU.mult, ALU.add))
                e.wait_ge(a_norm, 1)
                done(e.reciprocal(rstd[:, :], rstd[:, :]))

        def node_pass(name, normed, width, weights, tab, tw, evac, evac_count, w):
            vH, pT, aT, pY, vE = (sem(f"{x}_{name}") for x in ("v_in", "p_turn", "a_turn", "p_proj", "v_out"))
            s_st = [sem(f"s_{name}_store{i}") for i in range(2)]
            hs = w["hs"].rearrange("p (a c) -> p a c", a=2)
            hT = w["hT"].rearrange("p (a c) -> p a c", a=2)
            ob = w["ob"].rearrange("p (a t c) -> p a t c", a=2, t=GT)
            wide = GT * D
            tab_v = tab.rearrange("(t p) c -> p t c", p=P)

            @part("vector")
            def _(e):
                with e.Fori(0, NG // 2) as i:
                    for par in range(2):
                        n = 2 * i + par
                        t = bass.ds(n * GT, GT)
                        o = hs[:, par, :].rearrange("p (t d) -> p t d", t=GT)
                        if normed:
                            e.scalar_tensor_tensor(o, Y[:, t, :], 0.0, rstd[:, t].unsqueeze(2).to_broadcast([P, GT, D]),
                                                   ALU.max, ALU.mult).then_inc(vH, 1)
                        else:
                            move(e, o, Y[:, t, :]).then_inc(vH, 1)
                        e.wait_ge(pY, n + 1)
                        e.wait_ge(s_st[par], 16 * i)
                        k = [0]

                        def done(ins):
                            k[0] += 1
                            ins.then_inc(vE, 1)
                            e.wait_ge(vE, evac_count * n + k[0])
                        evac(e, t, ob[:, par], done)
                        assert k[0] == evac_count

            @part("tensor")
            def _(e):
                with e.Fori(0, NG // 2) as i:
                    for par in range(2):
                        n = 2 * i + par
                        e.wait_ge(vH, n + 1)
                        for j in range(GT):
                            ins = e.transpose(psum[0][:, j * D:(j + 1) * D], hs[:, par, j * D:(j + 1) * D], ident[:, :])
                        ins.then_inc(pT, 1)
                        e.wait_ge(aT, n + 1)
                        e.wait_ge(vE, evac_count * n)
                        for j in range(GT):
                            ins = e.matmul(psum[1 + j // 2][:, (j % 2) * 512:(j % 2) * 512 + width],
                                           hT[:, par, j * D:(j + 1) * D], weights, start=True, stop=True)
                        ins.then_inc(pY, 1)

            @part("scalar")
            def _(e):
                with e.Fori(0, NG // 2) as i:
                    for par in range(2):
                        n = 2 * i + par
                        e.wait_ge(pT, n + 1)
                        e.activation(hT[:, par, :], psum[0][:, 0:wide], ACT.Copy).then_inc(aT, 1)

            @part("sync")
            def _(e):
                with e.Fori(0, NG // 2) as i:
                    for par in range(2):
                        n = 2 * i + par
                        e.wait_ge(vE, evac_count * (n + 1))
                        e.dma_start(tab_v[:, bass.ds(n * GT, GT), :], ob[:, par, :, 0:tw]).then_inc(s_st[par], 16)
                for q in s_st:
                    e.wait_ge(q, 16 * (NG // 2))

        def proj(j0, j1, c0, c1):
            return psum[1 + j0 // 2][:, :].rearrange("p (j c) -> p j c", j=2)[:, 0:j1 - j0, c0:c1]

        PAIRS = [(0, 2), (2, 4), (4, 5)]

        def edge_pass(name, kind, H, C, tab, rw, idx, w, acc_w):
            soft = kind in ("gat", "hgt")
            GW = H * (C + 1) if soft else acc_w
            voff = D if kind == "hgt" else 0
            lw = {"gat": H, "hgt": D, "sum": D, "mean": 0}[kind]
            R = U * H
            acc = ACC[:, 0:NT * acc_w].rearrange("p (t c) -> p t c", c=acc_w)
            st = w["st"].bitcast(I32).rearrange("p (a v) -> p a v", a=2)
            g_ = w["g"].rearrange("p (a v c) -> p a v c", a=2, v=V)
            O = w["O"].rearrange("p (a v c) -> p a v c", a=2, v=V)
            s_idx, s_go = sem(f"a_{name}_idx"), sem(f"g_{name}_go")
            s_row = [swdge_sem(f"s_{name}_rows{i}") for i in range(2)]
            vA, pS, vG = sem(f"v_{name}_onehot"), sem(f"p_{name}_scatter"), sem(f"v_{name}_merge")
            vE = sem(f"v_{name}_msg")
            if lw:
                OT = w["OT"].rearrange("p (a v c) -> p a v c", a=2, v=V)
                pT, aT, pL = sem(f"p_{name}_turn"), sem(f"a_{name}_turn"), sem(f"p_{name}_lookup")
                psQ = psum[1][:, 0:V * lw].rearrange("p (v c) -> p v c", v=V)
            psS = psum[2][:, :].rearrange("p (u c) -> p u c", u=U)
            if soft:
                lo = w["lo"].rearrange("p (a c) -> p a c", a=2)
                dlr = w["dlr"].rearrange("p (a c) -> p a c", a=2)
                Rm = w["R"].rearrange("p (a v c) -> p a v c", a=2, v=V)
                pR, pB, pBb, vB, vC, vD, aX, vF, aW = (sem(f"{x}_{name}") for x in (
                    "p_rows", "p_cols", "p_cols_begun", "v_logits", "v_scans", "v_diff", "a_exp", "v_newmax", "a_scale"))
                psR = psum[3][:, 0:512].rearrange("p (a c) -> p a c", a=2)
                psB = psum[3][:, 512:512 + 3 * G * R].rearrange("p (a c) -> p a c", a=3)
                ne, fl, dr, fw, m, ml = (w[x] for x in ("ne", "fl", "dr", "fw", "m", "ml"))
                dif, ex, mk, mn, dd, ab, tmp = (w[x] for x in ("dif", "ex", "mk", "mn", "dd", "ab", "tmp"))
                CB, CC, CD, CF, CG = (2 if kind == "gat" else 2), 7, 2, 2 + 3 * U + 1, 1 + 2 * U
            elif kind == "sum":
                z = w["z"]
                rp, rn = w["rp"], w["rn"]
                Rm = w["R"].rearrange("p (a v c) -> p a v c", a=2, v=V)
                aT_attr = w["attr"].rearrange("p (a u c) -> p a u c", a=2, u=U)
                s_attr = [sem(f"s_{name}_attr{i}") for i in range(2)]
                vZ, aZ = sem(f"v_{name}_z"), sem(f"a_{name}_relu")
                CG = U
            else:
                CG = U
            out_w = GW + 2 * H if soft else acc_w

            def chunk(g, u):
                return g * U + u

            def act_idx(e, n, i, par):
                wait(e, s_row[par], 16 * V * i)
                e.activation(st[:, par, :], idx[:, bass.ds(n * V, V)], ACT.Copy).then_inc(s_idx, 1)

            def act_turn(e, n, i, par):
                e.wait_ge(pT, n + 1)
                wait(e, pL, n - 1)
                e.activation(OT[:, par].rearrange("p v c -> p (v c)"), psum[0][:, :], ACT.Copy).then_inc(aT, 1)

            def act_exp(e, n, i, par):
                e.wait_ge(vD, CD * n + CD)
                e.activation(ex, dif, ACT.Exp).then_inc(aX, 1)

            def act_scale(e, n, i, par):
                e.wait_ge(vF, CF * n + CF)
                e.activation(ab, dd, ACT.Exp).then_inc(aW, 1)

            def act_relu(e, n, i, par):
                e.wait_ge(vZ, n + 1)
                wait(e, vE, n)
                e.activation(rp, z, ACT.Relu).then_inc(aZ, 1)
                e.activation(rn, z, ACT.Relu, scale=-1.0).then_inc(aZ, 1)

            def pool_rows(e, n, i, par):
                e.wait_ge(s_idx, n + 1)
                if kind == "mean":
                    wait(e, pS, n - 1)
                else:
                    wait(e, vE, n - 1)
                e.sem_inc(s_go, 1)
                for v in range(V):
                    e.indirect_dma_start(g_[:, par, v, 0:rw], None, tab,
                                         bass.IndirectOffsetOnAxis(ap=st[:, par, v:v + 1], axis=0)
                                         ).then_inc(s_row[par], 16)

            def sync_attr(e, n, i, par):
                wait(e, pL, n - 1)
                bs = load_values(e, block_row, n, "block", NB - 1)
                for u in range(U):
                    e.dma_start(aT_attr[0:ATTRS, par, u, :], attr_t[:, bass.ds(bs[u] * EB, EB)]
                                ).then_inc(s_attr[par], 16)

            def pe_turn(e, n, i, par):
                e.wait_ge(vA, n + 1)
                wait(e, aT, n)
                for v in range(V):
                    ins = e.transpose(psum[0][:, v * P:(v + 1) * P], O[:, par, v, :], ident[:, :])
                ins.then_inc(pT, 1)

            def pe_lookup(e, n, i, par):
                ts = load_values(e, tile_row, n, "tile", NT - 1)
                e.wait_ge(aT, n + 1)
                if kind == "sum":
                    wait(e, vZ, n)
                    e.wait_ge(s_attr[par], 16 * U * (i + 1))
                else:
                    wait(e, vB, CB * n)
                for g in range(G):
                    for u in range(U):
                        v = chunk(g, u)
                        ins = e.matmul(psQ[:, v, :], OT[:, par, v, :],
                                       LK[:, bass.ds(ts[u], 1), 0:lw].rearrange("p t c -> p (t c)"),
                                       start=True, stop=kind != "sum")
                        if kind == "sum":
                            ins = e.matmul(psQ[:, v, :], aT_attr[0:ATTRS, par, u, g * P:(g + 1) * P],
                                           w["w_edge"][0:ATTRS, :], start=False, stop=True)
                ins.then_inc(pL, 1)

            def pe_rows(e, n, i, par):
                e.wait_ge(vB, CB * n + CB)
                wait(e, vC, CC * n)
                for a, t in ((0, lo), (1, dlr)):
                    for g in range(G):
                        ins = e.transpose(psR[0:R, a, g * P:(g + 1) * P], t[:, par, g * R:(g + 1) * R], ident[:, :])
                ins.then_inc(pR, 1)

            def pe_cols(e, n, i, par):
                e.wait_ge(vC, CC * n + CC)
                wait(e, vD, CD * n)
                e.sem_inc(pBb, 1)
                for a, t in ((0, m), (1, ml), (2, ne[:, 1:EB + 1])):
                    for g in range(G):
                        ins = e.transpose(psB[:, a, g * R:(g + 1) * R], t[0:R, g * P:(g + 1) * P], ident[0:R, 0:R])
                ins.then_inc(pB, 1)

            def pe_scatter(e, n, i, par):
                if kind == "mean":
                    e.wait_ge(vA, n + 1)
                    e.wait_ge(s_row[par], 16 * V * (i + 1))
                else:
                    e.wait_ge(vE, n + 1)
                wait(e, vG, CG * n)
                for u in range(U):
                    for g in range(G):
                        v = chunk(g, u)
                        rhs = g_[:, par, v, 0:out_w] if kind == "mean" else Rm[:, par, v, 0:out_w]
                        ins = e.matmul(psS[:, u, 0:out_w], O[:, par, v, :], rhs, start=g == 0, stop=g == G - 1)
                ins.then_inc(pS, 1)

            def dve_onehot(e, n, i, par):
                wait(e, pS, n - 1)
                cols = dst_c[:, bass.ds(n * V, V)]
                if soft:
                    d4 = dlr[:, par, :].rearrange("p (v h) -> p v h", h=H)
                    e.tensor_copy(d4, cols.unsqueeze(2).to_broadcast([P, V, H]))
                e.tensor_tensor(O[:, par], iota[:, :].unsqueeze(1).to_broadcast([P, V, P]),
                                cols.unsqueeze(2).to_broadcast([P, V, P]), ALU.is_equal).then_inc(vA, 1)

            def dve_logits(e, n, i, par):
                e.wait_ge(s_row[par], 16 * V * (i + 1))
                e.wait_ge(pL, n + 1)
                if kind == "gat":
                    l3 = lo[:, par, :].rearrange("p (v h) -> p v h", h=H)
                    e.tensor_tensor(l3, g_[:, par, :, GW:GW + H], psQ, ALU.add).then_inc(vB, 1)
                    e.wait_ge(vB, CB * n + 1)
                    e.scalar_tensor_tensor(lo[:, par, :], lo[:, par, :], 0.2, lo[:, par, :],
                                           ALU.mult, ALU.max).then_inc(vB, 1)
                else:
                    pr = w["prod"].rearrange("p (v c) -> p v c", v=V)
                    e.tensor_tensor(pr, g_[:, par, :, 0:D], psQ, ALU.mult).then_inc(vB, 1)
                    e.wait_ge(vB, CB * n + 1)
                    e.tensor_reduce(lo[:, par, :], w["prod"].rearrange("p (q c) -> p q c", c=C), AX.X,
                                    ALU.add).then_inc(vB, 1)

            def dve_scans(e, n, i, par):
                c = [0]

                def done(ins):
                    c[0] += 1
                    ins.then_inc(vC, 1)
                    e.wait_ge(vC, CC * n + c[0])
                e.wait_ge(pR, n + 1)
                wait(e, pB, n)
                r = slice(0, R)
                done(e.tensor_copy(dr[r, :], psR[r, 1, :]))
                done(e.tensor_tensor(ne[r, 1:EB], dr[r, 1:EB], dr[r, 0:EB - 1], ALU.not_equal))
                done(e.tensor_scalar(fl[r, :], ne[r, :], -BIG, None, ALU.mult))
                done(e.tensor_tensor_scan(fw[r, :], fl[r, 0:EB], psR[r, 0, :], -BIG, ALU.add, ALU.max))
                done(e.tensor_tensor_scan(m[r, ::-1], fl[r, 1:EB + 1][:, ::-1], fw[r, ::-1], -BIG,
                                          ALU.add, ALU.max))
                done(e.tensor_tensor(ml[r, :], m[r, :], ne[r, 1:EB + 1], ALU.mult))
                done(e.tensor_copy(dr[r, 0:1], ne[r, 0:1]))
                assert c[0] == CC

            def dve_diff(e, n, i, par):
                e.wait_ge(pB, n + 1)
                wait(e, aX, n)
                e.tensor_tensor(dif, lo[:, par, :], psB[:, 0, :], ALU.subtract).then_inc(vD, 1)
                o = Rm[:, par, :, GW:GW + 2 * H].rearrange("p v (q h) -> p q v h", q=2)
                e.tensor_copy(o, psB[:, 1:3, :].rearrange("p q (v h) -> p q v h", h=H)).then_inc(vD, 1)

            def dve_msg(e, n, i, par):
                if soft:
                    e.wait_ge(aX, n + 1)
                    x3 = ex.rearrange("p (v h) -> p v h", v=V).unsqueeze(3).to_broadcast([P, V, H, C + 1])
                    e.tensor_tensor(Rm[:, par, :, 0:GW].rearrange("p v (h c) -> p v h c", h=H),
                                    g_[:, par, :, voff:voff + GW].rearrange("p v (h c) -> p v h c", h=H),
                                    x3, ALU.mult).then_inc(vE, 1)
                elif kind == "sum":
                    e.wait_ge(aZ, 2 * n + 2)
                    wait(e, pS, n - 1)
                    e.scalar_tensor_tensor(Rm[:, par].rearrange("p v c -> p (v c)"), rn, w["neg_a"], rp,
                                           ALU.mult, ALU.add).then_inc(vE, 1)

            def dve_z(e, n, i, par):
                e.wait_ge(s_row[par], 16 * V * (i + 1))
                e.wait_ge(pL, n + 1)
                wait(e, aZ, 2 * n)
                e.tensor_tensor(z.rearrange("p (v c) -> p v c", v=V), g_[:, par], psQ, ALU.add).then_inc(vZ, 1)

            def dve_newmax(e, n, i, par):
                c = [0]

                def done(ins):
                    c[0] += 1
                    ins.then_inc(vF, 1)
                    e.wait_ge(vF, CF * n + c[0])
                ts = load_values(e, tile_row, n, "tile", NT - 1)
                e.wait_ge(pS, n + 1)
                wait(e, aW, n)
                mk3 = mk.rearrange("p (u h) -> p u h", u=U)
                mn3 = mn.rearrange("p (u h) -> p u h", u=U)
                dd4 = dd.rearrange("p (q u h) -> p q u h", q=2, u=U)
                done(e.tensor_scalar(mk3, psS[:, :, GW + H:GW + 2 * H], -1.0, BIG, ALU.add, ALU.mult))
                done(e.tensor_tensor(mk3, mk3, psS[:, :, GW:GW + H], ALU.add))
                for u in range(U):
                    mx = MX[:, bass.ds(ts[u], 1), 0:H].rearrange("p t h -> p (t h)")
                    done(e.tensor_tensor(mn3[:, u, :], mx, mk3[:, u, :], ALU.max))
                    done(e.tensor_tensor(dd4[:, 0, u, :], mx, mn3[:, u, :], ALU.subtract))
                    done(move(e, mx, mn3[:, u, :]))
                done(e.tensor_tensor(dd4[:, 1], mk3, mn3, ALU.subtract))
                return ts

            def dve_merge(e, n, i, par, ts):
                c = [0]

                def done(ins):
                    c[0] += 1
                    ins.then_inc(vG, 1)
                    e.wait_ge(vG, CG * n + c[0])
                if soft:
                    e.wait_ge(aW, n + 1)
                    ab4 = ab.rearrange("p (q u h) -> p q u h", q=2, u=U)
                    t4 = tmp.rearrange("p (u h c) -> p u h c", u=U, h=H)
                    done(e.tensor_tensor(t4, psS[:, :, 0:GW].rearrange("p u (h c) -> p u h c", h=H),
                                         ab4[:, 1].unsqueeze(3).to_broadcast([P, U, H, C + 1]), ALU.mult))
                    for u in range(U):
                        a3 = acc[:, bass.ds(ts[u], 1), :].rearrange("p t (h c) -> p (t h) c", h=H)
                        done(e.tensor_tensor(a3, a3, ab4[:, 0, u].unsqueeze(2).to_broadcast([P, H, C + 1]), ALU.mult))
                        done(e.tensor_tensor(a3, a3, t4[:, u], ALU.add))
                else:
                    ts = load_values(e, tile_row, n, "tile", NT - 1)
                    e.wait_ge(pS, n + 1)
                    for u in range(U):
                        a2 = acc[:, bass.ds(ts[u], 1), :].rearrange("p t c -> p (t c)")
                        done(e.tensor_tensor(a2, a2, psS[:, u, 0:acc_w], ALU.add))

            regs = {}

            def load_values(e, row, n, what, most):
                key = (id(e), what)
                if key not in regs:
                    regs[key] = [e.alloc_register(f"{name}_{what}{u}") for u in range(U)]
                e.load(regs[key], row[0:1, bass.ds(n * U, U)])
                return [e.snap(r, min_val=0, max_val=most) for r in regs[key]]

            def run(e, tick, lag):
                head, tail = 2 + lag + lag % 2, NI
                for n in range(head):
                    tick(n, n // 2, n % 2, False)
                with e.Fori(head // 2, tail // 2) as i:
                    for par in range(2):
                        tick(2 * i + par, i + 0, par, True)
                for n in range(tail, NI + lag):
                    tick(n, n // 2, n % 2, False)

            def stage(e, fn, lag, n, i, par, steady, *more):
                if not steady and not 0 <= n - lag < NI:
                    return None
                return fn(e, n - lag, i - (lag + 1 - par) // 2, (par - lag) % 2, *more)

            @part("sync")
            def _(e):
                if kind == "sum":
                    run(e, lambda *a: stage(e, sync_attr, 0, *a), 0)

            @part("gpsimd")
            def _(e):
                run(e, lambda *a: stage(e, pool_rows, 0, *a), 0)

            @part("scalar")
            def _(e):
                def tick(*a):
                    stage(e, act_idx, 0, *a)
                    if lw:
                        stage(e, act_turn, 0, *a)
                    if soft:
                        stage(e, act_exp, LX, *a)
                        stage(e, act_scale, LG, *a)
                    elif kind == "sum":
                        stage(e, act_relu, LX, *a)
                run(e, tick, LG if soft else LX if kind == "sum" else 0)

            @part("tensor")
            def _(e):
                def tick(*a):
                    if lw:
                        stage(e, pe_turn, 0, *a)
                    if soft:
                        stage(e, pe_lookup, 0, *a)
                        stage(e, pe_rows, LX, *a)
                        stage(e, pe_cols, LX, *a)
                    elif kind == "sum":
                        stage(e, pe_lookup, 0, *a)
                    stage(e, pe_scatter, LS, *a)
                run(e, tick, LS)

            @part("vector")
            def _(e):
                def tick(*a):
                    stage(e, dve_onehot, 0, *a)
                    if soft:
                        stage(e, dve_logits, LX, *a)
                        stage(e, dve_scans, LX, *a)
                        stage(e, dve_diff, LX, *a)
                        stage(e, dve_msg, LX, *a)
                        ts = stage(e, dve_newmax, LG, *a)
                        stage(e, dve_merge, LG, *a, ts)
                    else:
                        if kind == "sum":
                            stage(e, dve_z, LX, *a)
                            stage(e, dve_msg, LX, *a)
                        stage(e, dve_merge, LG, *a, None)
                run(e, tick, LG)

        LX = LS = LG = 0

        def edge_work(H, rw, C, soft, extra=()):
            GW = H * (C + 1)
            specs = [("st", 2 * V), ("g", 2 * V * rw), ("O", 2 * V * P), ("OT", 2 * V * P)]
            if soft:
                specs += [("R", 2 * V * (GW + 2 * H)), ("lo", 2 * V * H), ("dlr", 2 * V * H), ("ne", EB + 1),
                          ("fl", EB + 1), ("dr", EB), ("fw", EB), ("m", EB), ("ml", EB), ("dif", V * H),
                          ("ex", V * H), ("mk", U * H), ("mn", U * H), ("dd", 2 * U * H), ("ab", 2 * U * H),
                          ("tmp", U * GW)]
            return carve(specs + list(extra))

        def scan_ends(name, w):
            s = sem(f"v_{name}_ends")

            @part("vector")
            def _(e):
                e.memset(w["ne"], 1.0).then_inc(s, 1)
                e.wait_ge(s, 1)

        def gat_weights(name, Wm, Wt, a_s, a_d, H, w):
            C = D // H
            s_w, v_w_, p_w = sem(f"s_{name}_w"), sem(f"v_{name}_w"), sem(f"p_{name}_w")
            blk = w["blk"]

            @part("vector")
            def _(e):
                e.memset(blk[:, 0:2 * H], 0.0).then_inc(v_w_, 1)
                e.memset(w["ob"], 1.0).then_inc(v_w_, 1)
                e.wait_ge(v_w_, 2)
                e.wait_ge(p_w, 1)
                e.tensor_copy(w["W"][:, D:D + 2 * H], psum[0][:, 0:2 * H]).then_inc(v_w_, 1)
                e.wait_ge(v_w_, 3)

            @part("sync")
            def _(e):
                e.dma_start(w["W"][:, 0:D], Wm).then_inc(s_w, 16)
                e.dma_start(w["Wt"], Wt).then_inc(s_w, 16)
                e.wait_ge(v_w_, 1)
                for k, att in enumerate((a_s, a_d)):
                    for h in range(H):
                        e.dma_start(blk[h * C:(h + 1) * C, k * H + h:k * H + h + 1],
                                    att[h:h + 1, :].rearrange("a c -> c a"),
                                    allow_slow_non_contiguous=True).then_inc(s_w, 16)
                e.wait_ge(s_w, 16 * (2 + 2 * H))

            @part("tensor")
            def _(e):
                e.wait_ge(s_w, 16 * (2 + 2 * H))
                e.matmul(psum[0][:, 0:2 * H], w["Wt"], blk[:, 0:2 * H], start=True, stop=True).then_inc(p_w, 1)
                e.wait_ge(v_w_, 3)

        def gat_layer(name, normed, Wm, Wt, a_s, a_d, H, tab):
            C = D // H
            GW = H * (C + 1)
            TW = GW + H
            w = carve([("hs", 2 * GT * D), ("hT", 2 * GT * D), ("ob", 2 * GT * TW), ("W", D + 2 * H), ("Wt", D),
                       ("blk", 2 * H), ("sl", GT * H)])
            gat_weights(name, Wm, Wt, a_s, a_d, H, w)
            acc = ACC[:, 0:NT * GW].rearrange("p (t c) -> p t c", c=GW)

            def evac(e, t, ob, done):
                for a, b in PAIRS:
                    for j in range(a, b):
                        done(e.tensor_copy(ob[:, j, 0:GW].rearrange("p (h c) -> p h c", h=H)[:, :, 0:C],
                                           proj(j, j + 1, 0, D)[:, 0, :].rearrange("p (h c) -> p h c", h=H)
                                           if j % 2 == 0 else
                                           proj(j - 1, j + 1, 0, D)[:, 1, :].rearrange("p (h c) -> p h c", h=H)))
                    done(e.tensor_copy(ob[:, a:b, GW:TW], proj(a, b, D, D + H)))
                    done(e.tensor_copy(w["sl"].rearrange("p (t h) -> p t h", t=GT)[:, a:b],
                                       proj(a, b, D + H, D + 2 * H)))
                sl = w["sl"].rearrange("p (t h) -> p t h", t=GT)
                done(move(e, LK[:, t, 0:H], sl))
                done(e.tensor_tensor(sl, sl, ob[:, :, GW:TW], ALU.add))
                done(e.scalar_tensor_tensor(MX[:, t, 0:H], sl, 0.2, sl, ALU.mult, ALU.max))
                done(move(e, acc[:, t, :], ob[:, :, 0:GW]))
            node_pass(name, normed, D + 2 * H, w["W"], tab, TW, evac, GT + 2 * 3 + 4, w)
            meeting()
            we = edge_work(H, TW, C, True)
            scan_ends(name, we)
            edge_pass(name, "gat", H, C, tab, TW, src_c, we, GW)
            meeting()

        def chain(name):
            s = sem(f"v_{name}")
            n = [0]

            def begin(e):
                def done(ins):
                    n[0] += 1
                    ins.then_inc(s, 1)
                    e.wait_ge(s, n[0])
                return done
            return s, begin

        meeting()
        layer_norm("l0")
        gat_layer("gat1", True, W1, W1_t, att_src1, att_dst1, 4, tab_132)

        w = carve([("b1", D), ("rden", NT * 8)])
        s_b1 = sem("s_b1")
        s_neg, c_neg = chain("elu")
        a_elu = sem("a_elu")

        @part("sync")
        def _(e, w=w):
            e.dma_start(w["b1"], b1.partition_broadcast(P)).then_inc(s_b1, 16)
            e.wait_ge(s_b1, 16)

        @part("vector")
        def _(e, w=w):
            done = c_neg(e)
            H, C = 4, 32
            a4 = ACC[:, 0:NT * H * (C + 1)].rearrange("p (t h c) -> p t h c", h=H, c=C + 1)
            rd = w["rden"][:, 0:NT * H].rearrange("p (t h) -> p t h", h=H)
            done(e.tensor_scalar(rd.unsqueeze(3), a4[:, :, :, C:C + 1], 1e-16, None, ALU.add))
            done(e.reciprocal(rd, rd))
            done(e.tensor_tensor(Y[:, :, :].rearrange("p t (h c) -> p t h c", h=H), a4[:, :, :, 0:C],
                                 rd.unsqueeze(3).to_broadcast([P, NT, H, C]), ALU.mult))
            e.wait_ge(s_b1, 16)
            done(e.tensor_tensor(Y[:, :, :], Y[:, :, :], w["b1"].unsqueeze(1).to_broadcast([P, NT, D]), ALU.add))
            done(e.tensor_scalar(LK[:, :, :], Y[:, :, :], 0.0, None, ALU.min))
            e.wait_ge(a_elu, 1)
            done(e.scalar_tensor_tensor(Y[:, :, :], Y[:, :, :], 0.0, LK[:, :, :], ALU.max, ALU.add))
            done(e.tensor_scalar(Y[:, :, :], Y[:, :, :], -1.0, None, ALU.add))

        @part("scalar")
        def _(e, w=w):
            e.wait_ge(s_neg, 5)
            e.activation(LK[:, :, :], LK[:, :, :], ACT.Exp).then_inc(a_elu, 1)
        meeting()

        gat_layer("gat2", False, W2, W2_t, att_src2, att_dst2, 1, tab_129)

        w2_ = carve([("b2", D), ("rden", NT)])
        s_b2 = sem("s_b2")
        s_l2n, c_l2n = chain("l2norm")
        a_l2n = square_root("l2norm", w2_["rden"], s_l2n, 7)

        @part("sync")
        def _(e, w=w):
            e.dma_start(w2_["b2"], b2.partition_broadcast(P)).then_inc(s_b2, 16)
            e.wait_ge(s_b2, 16)

        @part("vector")
        def _(e, w=w):
            done = c_l2n(e)
            a3 = ACC[:, 0:NT * (D + 1)].rearrange("p (t c) -> p t c", c=D + 1)
            rd = w2_["rden"].unsqueeze(2)
            big = [P, NT, D]
            done(e.tensor_scalar(rd, a3[:, :, D:D + 1], 1e-16, None, ALU.add))
            done(e.reciprocal(rd, rd))
            done(e.tensor_tensor(Y[:, :, :], a3[:, :, 0:D], rd.to_broadcast(big), ALU.mult))
            e.wait_ge(s_b2, 16)
            done(e.tensor_tensor(Y[:, :, :], Y[:, :, :], w2_["b2"].unsqueeze(1).to_broadcast(big), ALU.add))
            done(e.tensor_tensor(LK[:, :, :], Y[:, :, :], Y[:, :, :], ALU.mult))
            done(e.tensor_reduce(w2_["rden"], LK[:, :, :], AX.X, ALU.add))
            done(e.tensor_scalar(w2_["rden"], w2_["rden"], 1e-24, None, ALU.max))
            e.wait_ge(a_l2n, 1)
            done(e.reciprocal(w2_["rden"], w2_["rden"]))
            done(e.tensor_tensor(Y[:, :, :], Y[:, :, :], rd.to_broadcast(big), ALU.mult))
            done(e.tensor_tensor(X[:, :, :], X[:, :, :], Y[:, :, :], ALU.add))
        meeting()

        layer_norm("l1")
        w = carve([("hs", 2 * GT * D), ("hT", 2 * GT * D), ("ob", 2 * GT * D), ("W", 2 * D), ("bias", 3 * D)])
        s_w1 = sem("s_l1_w")
        s_w1v, c_w1 = chain("l1_bias")

        @part("sync")
        def _(e, w=w):
            e.dma_start(w["W"][:, 0:D], w_src_t).then_inc(s_w1, 16)
            e.dma_start(w["W"][:, D:2 * D], w_dst_t).then_inc(s_w1, 16)
            for k, b in enumerate((b_src, b_dst, b_edge)):
                e.dma_start(w["bias"][:, k * D:(k + 1) * D], b.partition_broadcast(P)).then_inc(s_w1, 16)
            e.wait_ge(s_w1, 80)

        @part("tensor")
        def _(e, w=w):
            e.wait_ge(s_w1, 80)

        @part("vector")
        def _(e, w=w):
            done = c_w1(e)
            e.wait_ge(s_w1, 80)
            b = w["bias"]
            done(e.tensor_tensor(b[:, 0:D], b[:, 0:D], b[:, D:2 * D], ALU.add))
            done(e.tensor_tensor(b[:, 0:D], b[:, 0:D], b[:, 2 * D:3 * D], ALU.add))

        def evac_pair(w, ones_col):
            def evac(e, t, ob, done):
                for a, b in PAIRS:
                    done(e.tensor_copy(ob[:, a:b, 0:D], proj(a, b, 0, D)))
                    done(e.tensor_tensor(w["ev"].rearrange("p (t c) -> p t c", t=GT)[:, a:b], proj(a, b, D, 2 * D),
                                         w["bias"][:, 0:D].unsqueeze(1).to_broadcast([P, b - a, D]), ALU.add))
                done(move(e, LK[:, t, :], w["ev"].rearrange("p (t c) -> p t c", t=GT)))
            return evac
        w["ev"] = work[:, 12000:12000 + GT * D]
        node_pass("l1", True, 2 * D, w["W"], tab_sum, D, evac_pair(w, False), 7, w)
        meeting()
        w = edge_work(1, D, D, False, [("z", V * D), ("rp", V * D), ("rn", V * D), ("R", 2 * V * D),
                                       ("attr", 2 * U * EB), ("w_edge", D), ("neg_a", 1)])
        s_we = sem("s_l1_we")
        s_we_v, c_we = chain("l1_nega")

        @part("sync")
        def _(e, w=w):
            e.dma_start(w["w_edge"][0:ATTRS, :], w_edge_t).then_inc(s_we, 16)
            e.dma_start(w["neg_a"], prelu_a.partition_broadcast(P)).then_inc(s_we, 16)
            e.wait_ge(s_we, 32)

        @part("tensor")
        def _(e, w=w):
            e.wait_ge(s_we, 32)

        @part("vector")
        def _(e, w=w):
            done = c_we(e)
            e.wait_ge(s_we, 32)
            done(e.tensor_scalar(w["neg_a"], w["neg_a"], -1.0, None, ALU.mult))
            done(e.memset(ACC[:, 0:NT * D], 0.0))
        edge_pass("l1", "sum", 1, D, tab_sum, D, src_c, w, D)
        meeting()

        w = carve([("gamma", D), ("beta", D), ("a", 1), ("part", D), ("part2", D), ("mean", D), ("rs", D)])
        s_bn = sem("s_bn")
        s_bnv, c_bn = chain("bn")
        a_bn = square_root("bn", w["rs"], s_bnv, 6)
        p_bn = sem("p_bn")

        @part("sync")
        def _(e, w=w):
            for k, (t, b) in enumerate((("gamma", gamma), ("beta", beta), ("a", prelu_a))):
                e.dma_start(w[t], b.partition_broadcast(P)).then_inc(s_bn, 16)
            e.wait_ge(s_bn, 48)

        @part("vector")
        def _(e, w=w):
            done = c_bn(e)
            a3 = ACC[:, 0:NT * D].rearrange("p (t c) -> p t c", c=D)
            big = [P, NT, D]
            done(e.tensor_reduce(w["part"], a3[:, 0:NODE_TILES, :].rearrange("p t c -> p c t"), AX.X, ALU.add))
            e.wait_ge(p_bn, 1)
            done(e.tensor_scalar(w["mean"], psum[0][:, 0:D], 1.0 / N, None, ALU.mult))
            done(e.tensor_tensor(Y[:, :, :], a3, w["mean"].unsqueeze(1).to_broadcast(big), ALU.subtract))
            done(e.tensor_tensor(LK[:, :, :], Y[:, :, :], Y[:, :, :], ALU.mult))
            done(e.tensor_reduce(w["part2"], LK[:, 0:NODE_TILES - 1, :].rearrange("p t c -> p c t"), AX.X, ALU.add))
            e.wait_ge(p_bn, 2)
            done(e.tensor_scalar(w["rs"], psum[1][:, 0:D], 1.0 / N, 1e-5, ALU.mult, ALU.add))
            e.wait_ge(a_bn, 1)
            done(e.reciprocal(w["rs"], w["rs"]))
            e.wait_ge(s_bn, 48)
            done(e.tensor_tensor(w["rs"], w["rs"], w["gamma"], ALU.mult))
            done(e.tensor_tensor(Y[:, :, :], Y[:, :, :], w["rs"].unsqueeze(1).to_broadcast(big), ALU.mult))
            done(e.tensor_tensor(Y[:, :, :], Y[:, :, :], w["beta"].unsqueeze(1).to_broadcast(big), ALU.add))
            done(e.tensor_scalar(LK[:, :, :], Y[:, :, :], 0.0, w["a"], ALU.min, ALU.mult))
            done(e.scalar_tensor_tensor(Y[:, :, :], Y[:, :, :], 0.0, LK[:, :, :], ALU.max, ALU.add))
            done(e.tensor_tensor(X[:, :, :], X[:, :, :], Y[:, :, :], ALU.add))

        @part("tensor")
        def _(e, w=w):
            e.wait_ge(s_bnv, 1)
            e.matmul(psum[0][:, 0:D], ones[:, :], w["part"], start=True, stop=True).then_inc(p_bn, 1)
            e.wait_ge(s_bnv, 5)
            e.matmul(psum[1][:, 0:D], ones[:, :], w["part2"], start=True, stop=False)
            e.matmul(psum[1][:, 0:D], ones[0:TAIL, :], LK[0:TAIL, NODE_TILES - 1, :],
                     start=False, stop=True).then_inc(p_bn, 1)
        meeting()

        HH, HC = 8, 16
        layer_norm("l2")
        meeting()
        ntb = ACC[:, 0:NT * D]
        nt_nat = MX
        RW = RELS * ROW
        OBW = 17 * 8 + D
        w = carve([("hs", GT * D), ("hT", GT * D), ("hm", 2 * GT * D), ("kv", 2 * GT * D), ("wt", 3 * TYPES * D),
                   ("bd", 2 * RELS * D), ("ob", 2 * RW), ("prib", RELS * HH)])
        s_hw = sem("s_hgt_w")
        s_hwv, c_hw = chain("hgt_w")
        wt = w["wt"].rearrange("p (q t c) -> p q t c", q=3, t=TYPES)
        bd = w["bd"].rearrange("p (q r c) -> p q r c", q=2, r=RELS)
        hob = w["ob"].rearrange("p (a r c) -> p a r c", a=2, r=RELS)
        HW_N = 3 + 1 + 2 * HH + 1

        @part("sync")
        def _(e, w=w):
            for q, t in enumerate((k_w, v_w, q_w)):
                e.dma_start(wt[:, q], t.rearrange("t i o -> i t o")).then_inc(s_hw, 16)
            e.dma_start(w["prib"], pri.rearrange("r h -> (r h)").partition_broadcast(P)).then_inc(s_hw, 16)
            e.wait_ge(s_hwv, 1)
            for q, t in enumerate((rel_att, rel_msg)):
                for h in range(HH):
                    e.dma_start(bd[h * HC:(h + 1) * HC, q, :, h * HC:(h + 1) * HC],
                                t[:, h].rearrange("r d c -> d r c")).then_inc(s_hw, 16)
            e.dma_start(ntb.bitcast(I32), node_type.partition_broadcast(P)).then_inc(s_hw, 16)
            e.wait_ge(s_hw, 16 * HW_N)

        @part("tensor")
        def _(e, w=w):
            e.wait_ge(s_hw, 16 * HW_N)

        @part("vector")
        def _(e, w=w):
            done = c_hw(e)
            done(e.memset(w["bd"], 0.0))
            done(e.memset(w["ob"], 1.0))
            e.wait_ge(s_hw, 16 * HW_N)
            done(e.tensor_scalar(w["prib"], w["prib"], float(D) ** -0.5, None, ALU.mult))
            done(e.tensor_tensor(bd[:, 0].rearrange("p r (h c) -> p (r h) c", h=HH),
                                 bd[:, 0].rearrange("p r (h c) -> p (r h) c", h=HH),
                                 w["prib"].unsqueeze(2).to_broadcast([P, RELS * HH, HC]), ALU.mult))
            done(e.tensor_copy(ntb, ntb.bitcast(I32)))

        vN, pN, aN, vM, pP, aK, pQ2, vK, pRl, vRl, aRl = (sem(f"{x}_hgt") for x in (
            "v_in", "p_turn", "a_turn", "v_mask", "p_typed", "a_kv", "p_typed_use", "v_q", "p_rel", "v_rel", "a_rel"))
        s_ob = [sem(f"s_hgt_store{i}") for i in range(2)]
        tabr = tab_rel.rearrange("(t p r) c -> t p (r c)", p=P, r=RELS)
        RB = RELS // 4
        JR = GT * RB

        @part("vector")
        def _(e, w=w):
            with e.Fori(0, NG) as n:
                t = bass.ds(n * GT, GT)
                wait_n(e, pN, n)
                e.scalar_tensor_tensor(w["hs"].rearrange("p (t d) -> p t d", t=GT), Y[:, t, :], 0.0,
                                       rstd[:, t].unsqueeze(2).to_broadcast([P, GT, D]),
                                       ALU.max, ALU.mult).then_inc(vN, 1)
                e.wait_ge(aN, n + 1)
                hm = w["hm"].rearrange("p (a c) -> p a c", a=2)
                for ty in range(TYPES):
                    e.wait_ge(pP, n * TYPES + max(ty - 1, 0))
                    e.scalar_tensor_tensor(hm[:, ty % 2, :], ntb[:, bass.ds(n * (GT * D), GT * D)], float(ty),
                                           w["hT"], ALU.is_equal, ALU.mult).then_inc(vM, 1)
                e.wait_ge(pP, n * TYPES + TYPES)
                move(e, LK[:, t, :], psum[3][:, 0:GT * D].rearrange("p (t c) -> p t c", t=GT)).then_inc(vK, 1)
                for j in range(GT):
                    for rb in range(RB):
                        e.wait_ge(pRl, 2 * JR * n + 2 * (j * RB + rb) + 2)
                        if rb == 0:
                            wait_ob(e, n, j)
                        o = hob4(j)[:, rb * 4:rb * 4 + 4, D:D + 17 * HH].rearrange(
                            "p r (h c) -> p r h c", h=HH)[:, :, :, 0:HC]
                        for r in range(4):
                            ins = e.tensor_copy(o[:, r], psum[0][:, 512 + r * D:512 + (r + 1) * D].rearrange(
                                "p (h c) -> p h c", h=HH))
                        ins.then_inc(vRl, 1)

        def wait_n(e, s, v):
            e.wait_ge(s, v)

        def hob4(j):
            return hob[:, j % 2]

        def wait_ob(e, n, j):
            per = (GT + 1 - j % 2) // 2
            e.wait_ge(s_ob[j % 2], (n * per + j // 2) * 16)

        @part("tensor")
        def _(e, w=w):
            hm = w["hm"].rearrange("p (a c) -> p a c", a=2)
            kv = w["kv"].rearrange("p (a c) -> p a c", a=2)
            wide = GT * D
            with e.Fori(0, NG) as n:
                e.wait_ge(vN, n + 1)
                e.wait_ge(vRl, JR * n)
                e.wait_ge(aRl, JR * n)
                for j in range(GT):
                    ins = e.transpose(psum[0][:, j * D:(j + 1) * D], w["hs"][:, j * D:(j + 1) * D], ident[:, :])
                ins.then_inc(pN, 1)
                e.wait_ge(aK, 2 * n)
                e.wait_ge(vK, n)
                for ty in range(TYPES):
                    e.wait_ge(vM, n * TYPES + ty + 1)
                    first, last = ty == 0, ty == TYPES - 1
                    for q in range(2):
                        for a, b in ((0, 512), (512, wide)):
                            e.matmul(psum[1 + q][:, a:b], wt[:, q, ty, :], hm[:, ty % 2, a:b], start=first, stop=last)
                    for j in range(GT):
                        ins = e.matmul(psum[3][:, j * D:(j + 1) * D], hm[:, ty % 2, j * D:(j + 1) * D],
                                       wt[:, 2, ty, :], start=first and j % 4 == 0, stop=last, skip_group_check=True)
                    ins.then_inc(pP, 1)
                e.wait_ge(aK, 2 * n + 2)
                for j in range(GT):
                    for rb in range(RB):
                        k = j * RB + rb
                        for q in range(2):
                            if q == 0:
                                e.wait_ge(aRl, JR * n + k)
                            else:
                                e.wait_ge(vRl, JR * n + k)
                            e.matmul(psum[0][:, q * 512:(q + 1) * 512], kv[:, q, j * D:(j + 1) * D],
                                     bd[:, q, rb * 4:rb * 4 + 4, :], start=True, stop=True).then_inc(pRl, 1)

        @part("scalar")
        def _(e, w=w):
            kv = w["kv"].rearrange("p (a c) -> p a c", a=2)
            wide = GT * D
            with e.Fori(0, NG) as n:
                e.wait_ge(pN, n + 1)
                e.activation(w["hT"], psum[0][:, 0:wide], ACT.Copy).then_inc(aN, 1)
                e.wait_ge(pP, n * TYPES + TYPES)
                for q in range(2):
                    e.activation(kv[:, q, :], psum[1 + q][:, 0:wide], ACT.Copy).then_inc(aK, 1)
                for j in range(GT):
                    for rb in range(RB):
                        e.wait_ge(pRl, 2 * JR * n + 2 * (j * RB + rb) + 1)
                        if rb == 0:
                            wait_ob(e, n, j)
                        e.activation(hob4(j)[:, rb * 4:rb * 4 + 4, 0:D],
                                     psum[0][:, 0:512].rearrange("p (r c) -> p r c", r=4), ACT.Copy).then_inc(aRl, 1)

        @part("sync")
        def _(e, w=w):
            with e.Fori(0, NG) as n:
                for j in range(GT):
                    e.wait_ge(vRl, JR * n + (j + 1) * RB)
                    e.wait_ge(aRl, JR * n + (j + 1) * RB)
                    e.dma_start(tabr[bass.ds(n * GT + j, 1)].rearrange("t p c -> p (t c)"),
                                hob4(j).rearrange("p r c -> p (r c)")).then_inc(s_ob[j % 2], 16)
            e.wait_ge(s_ob[0], 16 * 3 * NG)
            e.wait_ge(s_ob[1], 16 * 2 * NG)
        meeting()

        w = edge_work(HH, OBW, HC, True, [("prod", V * D)])
        scan_ends("hgt", w)
        s_hz, c_hz = chain("hgt_zero")

        @part("vector")
        def _(e, w=w):
            done = c_hz(e)
            done(e.memset(ACC[:, :], 0.0))
            done(e.memset(MX[:, :, :], -BIG))
        edge_pass("hgt", "hgt", HH, HC, tab_rel, OBW, rel_c, w, HH * (HC + 1))
        meeting()

        w = carve([("rden", NT * HH), ("gate", NT * HH), ("gt", NT * HH), ("sk", TYPES * HH), ("ntc", NT),
                   ("oht", NT), ("wa", TYPES * D), ("hs", GT * D), ("hT", GT * D), ("hm", 2 * GT * D), ("nti", NT)])
        s_sk = sem("s_skip")
        s_tv, c_tv = chain("hgt_end")
        a_sk = sem("a_skip")
        vn2, pn2, an2, vm2, pp2, vx2 = (sem(f"{x}_hgtout") for x in (
            "v_in", "p_turn", "a_turn", "v_mask", "p_typed", "v_out"))
        wa = w["wa"].rearrange("p (t c) -> p t c", t=TYPES)

        @part("sync")
        def _(e, w=w):
            e.dma_start(wa, a_w.rearrange("t i o -> i t o")).then_inc(s_sk, 16)
            e.dma_start(w["sk"], skip.rearrange("t h -> (t h)").partition_broadcast(P)).then_inc(s_sk, 16)
            e.dma_start(w["nti"].bitcast(I32), node_type.rearrange("(t p) -> p t", p=P),
                        allow_slow_non_contiguous=True).then_inc(s_sk, 16)
            e.wait_ge(s_tv, 4)
            e.dma_start(ntb.bitcast(I32), node_type.partition_broadcast(P)).then_inc(s_sk, 16)
            e.wait_ge(s_sk, 64)

        @part("tensor")
        def _(e, w=w):
            e.wait_ge(s_sk, 64)

        @part("scalar")
        def _(e, w=w):
            e.wait_ge(s_sk, 64)
            e.activation(w["sk"], w["sk"], ACT.Exp, scale=-1.0).then_inc(a_sk, 1)

        @part("vector")
        def _(e, w=w):
            done = c_tv(e)
            a4 = ACC[:, 0:NT * HH * (HC + 1)].rearrange("p (t h c) -> p t h c", h=HH, c=HC + 1)
            rd = w["rden"].rearrange("p (t h) -> p t h", h=HH)
            done(e.tensor_scalar(rd.unsqueeze(3), a4[:, :, :, HC:HC + 1], 1e-30, None, ALU.max))
            done(e.reciprocal(rd, rd))
            done(e.tensor_tensor(Y[:, :, :].rearrange("p t (h c) -> p t h c", h=HH), a4[:, :, :, 0:HC],
                                 rd.unsqueeze(3).to_broadcast([P, NT, HH, HC]), ALU.mult))
            done(e.memset(w["gate"], 0.0))
            e.wait_ge(a_sk, 1)
            e.wait_ge(s_sk, 64)
            done(e.tensor_scalar(w["sk"], w["sk"], 1.0, None, ALU.add))
            done(e.reciprocal(w["sk"], w["sk"]))
            done(e.tensor_copy(w["ntc"], w["nti"].bitcast(I32)))
            done(e.tensor_copy(ntb, ntb.bitcast(I32)))
            sk = w["sk"].rearrange("p (t h) -> p t h", h=HH)
            gt = w["gt"].rearrange("p (t h) -> p t h", h=HH)
            for ty in range(TYPES):
                done(e.tensor_scalar(w["oht"], w["ntc"], float(ty), None, ALU.is_equal))
                done(e.tensor_tensor(gt, w["oht"].unsqueeze(2).to_broadcast([P, NT, HH]),
                                     sk[:, ty:ty + 1, :].to_broadcast([P, NT, HH]), ALU.mult))
                done(e.tensor_tensor(w["gate"], w["gate"], w["gt"], ALU.add))
            hm = w["hm"].rearrange("p (a c) -> p a c", a=2)
            gate = w["gate"].rearrange("p (t h) -> p t h", h=HH)
            with e.Fori(0, NG) as n:
                t = bass.ds(n * GT, GT)
                move(e, w["hs"].rearrange("p (t d) -> p t d", t=GT), Y[:, t, :]).then_inc(vn2, 1)
                e.wait_ge(an2, n + 1)
                for ty in range(TYPES):
                    e.wait_ge(pp2, n * TYPES + max(ty - 1, 0))
                    e.scalar_tensor_tensor(hm[:, ty % 2, :], ntb[:, bass.ds(n * (GT * D), GT * D)], float(ty),
                                           w["hT"], ALU.is_equal, ALU.mult).then_inc(vm2, 1)
                e.wait_ge(pp2, n * TYPES + TYPES)
                for h in range(HH):
                    e.wait_ge(vn2, n + 1)
                    ins = e.tensor_tensor(Y[:, t, h * HC:(h + 1) * HC],
                                          psum[1][:, 0:GT * D].rearrange("p (t c) -> p t c", t=GT)[
                                              :, :, h * HC:(h + 1) * HC],
                                          gate[:, t, h:h + 1].to_broadcast([P, GT, HC]), ALU.mult)
                ins.then_inc(vx2, 1)
            e.wait_ge(vx2, NG)
            done(e.tensor_tensor(X[:, :, :], X[:, :, :], Y[:, :, :], ALU.add))

        @part("tensor")
        def _(e, w=w):
            hm = w["hm"].rearrange("p (a c) -> p a c", a=2)
            with e.Fori(0, NG) as n:
                e.wait_ge(vn2, n + 1)
                for j in range(GT):
                    ins = e.transpose(psum[0][:, j * D:(j + 1) * D], w["hs"][:, j * D:(j + 1) * D], ident[:, :])
                ins.then_inc(pn2, 1)
                e.wait_ge(vx2, n)
                for ty in range(TYPES):
                    e.wait_ge(vm2, n * TYPES + ty + 1)
                    for j in range(GT):
                        ins = e.matmul(psum[1][:, j * D:(j + 1) * D], hm[:, ty % 2, j * D:(j + 1) * D], wa[:, ty, :],
                                       start=ty == 0 and j % 4 == 0, stop=ty == TYPES - 1, skip_group_check=True)
                    ins.then_inc(pp2, 1)

        @part("scalar")
        def _(e, w=w):
            with e.Fori(0, NG) as n:
                e.wait_ge(pn2, n + 1)
                e.activation(w["hT"], psum[0][:, 0:GT * D], ACT.Copy).then_inc(an2, 1)
        meeting()

        layer_norm("l3")
        w = carve([("hs", 2 * GT * D), ("hT", 2 * GT * D), ("ob", 2 * GT * (D + 1)), ("W", 2 * D), ("bias", D),
                   ("ev", GT * D)])
        s_w3 = sem("s_l3_w")
        s_w3v, c_w3 = chain("l3_ones")

        @part("sync")
        def _(e, w=w):
            e.dma_start(w["W"][:, 0:D], W3_t[D:2 * D, :]).then_inc(s_w3, 16)
            e.dma_start(w["W"][:, D:2 * D], W3_t[0:D, :]).then_inc(s_w3, 16)
            e.dma_start(w["bias"], b3.partition_broadcast(P)).then_inc(s_w3, 16)
            e.wait_ge(s_w3, 48)

        @part("tensor")
        def _(e, w=w):
            e.wait_ge(s_w3, 48)

        @part("vector")
        def _(e, w=w):
            done = c_w3(e)
            e.wait_ge(s_w3, 48)
            done(e.memset(w["ob"], 1.0))
        node_pass("l3", True, 2 * D, w["W"], tab_mean, D + 1, evac_pair(w, True), 7, w)
        meeting()
        w = edge_work(1, D + 1, D, False)
        s_mz, c_mz = chain("l3_zero")

        @part("vector")
        def _(e, w=w):
            done = c_mz(e)
            done(e.memset(ACC[:, :], 0.0))
        edge_pass("l3", "mean", 1, D, tab_mean, D + 1, src_c, w, D + 1)
        meeting()

        w = carve([("cnt", NT)])
        s_fin, c_fin = chain("final")
        s_out = sem("s_out")

        @part("vector")
        def _(e, w=w):
            done = c_fin(e)
            a3 = ACC[:, 0:NT * (D + 1)].rearrange("p (t c) -> p t c", c=D + 1)
            cnt = w["cnt"].unsqueeze(2)
            done(e.tensor_scalar(cnt, a3[:, :, D:D + 1], 1.0, None, ALU.max))
            done(e.reciprocal(w["cnt"], w["cnt"]))
            done(e.tensor_tensor(Y[:, :, :], a3[:, :, 0:D], cnt.to_broadcast([P, NT, D]), ALU.mult))
            done(e.tensor_tensor(Y[:, :, :], Y[:, :, :], LK[:, :, :], ALU.add))
            done(e.tensor_tensor(X[:, :, :], X[:, :, :], Y[:, :, :], ALU.add))

        @part("sync")
        def _(e, w=w):
            e.wait_ge(s_fin, 5)
            full = (NODE_TILES - 1) * P
            e.dma_start(out[0:full, :].rearrange("(t p) d -> p t d", p=P), X[:, 0:NODE_TILES - 1, :]
                        ).then_inc(s_out, 16)
            e.dma_start(out[full:N, :], X[0:TAIL, NODE_TILES - 1, :]).then_inc(s_out, 16)
            e.wait_ge(s_out, 32)

        block = ctx.enter_context(nc.Block())

        @block.sync
        def _(e):
            for f in parts["sync"]:
                f(e)

        @block.gpsimd
        def _(e):
            for f in parts["gpsimd"]:
                f(e)

        @block.scalar
        def _(e):
            for f in parts["scalar"]:
                f(e)

        @block.vector
        def _(e):
            for f in parts["vector"]:
                f(e)

        @block.tensor
        def _(e):
            for f in parts["tensor"]:
                f(e)


def kernel(**inputs):
    from concourse import bacc
    from concourse.bass_utils import run_bass_kernel_spmd

    a = {k: np.asarray(v) for k, v in inputs.items()}

    def filled(v, rows, fill):
        return np.concatenate([v, np.full((rows - v.shape[0],) + v.shape[1:], fill, v.dtype)])

    arrays = {
        "src_rows": filled(a["src"], NB * EB, 0).reshape(NB, EB),
        "dst_rows": filled(a["dst"], NB * EB, PAD_DST).reshape(NB, EB),
        "etype_rows": filled(a["edge_type_16"], NB * EB, 0).reshape(NB, EB),
        "attr_t": np.ascontiguousarray(filled(a["edge_attr_17"], NB * EB, 0).T),
        "x": np.ascontiguousarray(filled(a["x"], NP, 0).reshape(NT, P, D).transpose(1, 0, 2)),
        "node_type": filled(a["node_type_8"], NP, 0),
        "W1": a["L0_gnn_W1"], "att_src1": a["L0_gnn_att_src1"], "att_dst1": a["L0_gnn_att_dst1"],
        "b1": a["L0_gnn_b1"], "W2": a["L0_gnn_W2"], "att_src2": a["L0_gnn_att_src2"],
        "att_dst2": a["L0_gnn_att_dst2"], "b2": a["L0_gnn_b2"],
        "w_src_t": np.ascontiguousarray(a["L1_gnn_W_src"].T), "b_src": a["L1_gnn_b_src"],
        "w_dst_t": np.ascontiguousarray(a["L1_gnn_W_dst"].T), "b_dst": a["L1_gnn_b_dst"],
        "w_edge_t": np.ascontiguousarray(a["L1_gnn_W_edge"].T), "b_edge": a["L1_gnn_b_edge"],
        "prelu_a": a["L1_gnn_prelu_a"].reshape(1), "gamma": a["L1_gnn_gamma"], "beta": a["L1_gnn_beta"],
        "k_w": a["L2_gnn_k_weight"], "q_w": a["L2_gnn_q_weight"], "v_w": a["L2_gnn_v_weight"],
        "a_w": a["L2_gnn_a_weight"], "pri": a["L2_gnn_relation_pri"], "rel_att": a["L2_gnn_relation_att"],
        "rel_msg": a["L2_gnn_relation_msg"], "skip": a["L2_gnn_skip"],
        "W3_t": np.ascontiguousarray(a["L3_gnn_W"].T), "b3": a["L3_gnn_b"],
        "W1_t": np.ascontiguousarray(a["L0_gnn_W1"].T), "W2_t": np.ascontiguousarray(a["L0_gnn_W2"].T),
    }
    nc = bacc.Bacc("TRN2", target_bir_lowering=False, num_devices=1)
    args = {}
    for name, v in arrays.items():
        args[name] = nc.dram_tensor(f"in_{name}", v.shape, mybir.dt.from_np(v.dtype), kind="ExternalInput").ap()
    out = nc.dram_tensor("out_x", (N, D), F32, kind="ExternalOutput").ap()
    build(nc, out=out, **args)
    r = run_bass_kernel_spmd(nc, [{f"in_{k}": v for k, v in arrays.items()}], core_ids=[0])
    return r.results[0]["out_x"]
```
